# Optimizing a Trainium2 kernel written in Bass

```python
import numpy as np
import jax
import jax.numpy as jnp

def _softmax(x, axis=-1):
    return jax.nn.softmax(x, axis=axis)

def _gelu(x):
    return jax.nn.gelu(x, approximate=True)

def _silu(x):
    return jax.nn.silu(x)

def _sigmoid(x):
    return jax.nn.sigmoid(x)

def _layernorm(x, axis=-1, eps=1e-05):
    m = jnp.mean(x, axis=axis, keepdims=True)
    v = jnp.var(x, axis=axis, keepdims=True)
    return (x - m) / jnp.sqrt(v + eps)

def _scatter_add(tgt, idx, src, axis=0):
    return tgt.at[idx].add(src)

def _segment_sum(src, seg, n):
    return jax.ops.segment_sum(src, seg, n)
kernel_name = 'mk_dlrm_tower_d1_rec_r8_1eb9c9'

def setup_inputs(seed: int=0):
    np.random.seed(seed)
    _w = jnp.asarray

    def _rec_inputs():
        import jax
        import jax.numpy as jnp
        _tk = jax.random.key(seed)
        dense_ctx = jax.random.normal(jax.random.fold_in(_tk, 190), (1024, 16), jnp.float32)
        ids = jnp.stack([jax.random.randint(jax.random.fold_in(_tk, 200 + f), (1024,), 0, v, jnp.int32) for f, v in enumerate([125000, 1000, 1000, 125000, 1000, 125000, 12500, 1250, 1250, 125000, 1000, 1000, 12500, 12500, 12500, 1000, 1250, 125000, 1000, 1000, 125000, 1000, 125000, 1000, 125000, 125000, 12500, 1000, 1000, 125000, 1000, 12500, 1250, 12500, 125000, 12500, 12500, 125000, 125000])], axis=1)
        tbl_0 = 0.05 * jax.random.normal(jax.random.fold_in(_tk, 500 + 0), (125000, 16), jnp.float32)
        tbl_1 = 0.05 * jax.random.normal(jax.random.fold_in(_tk, 500 + 1), (1000, 16), jnp.float32)
        tbl_2 = 0.05 * jax.random.normal(jax.random.fold_in(_tk, 500 + 2), (1000, 16), jnp.float32)
        tbl_3 = 0.05 * jax.random.normal(jax.random.fold_in(_tk, 500 + 3), (125000, 16), jnp.float32)
        tbl_4 = 0.05 * jax.random.normal(jax.random.fold_in(_tk, 500 + 4), (1000, 16), jnp.float32)
        tbl_5 = 0.05 * jax.random.normal(jax.random.fold_in(_tk, 500 + 5), (125000, 16), jnp.float32)
        tbl_6 = 0.05 * jax.random.normal(jax.random.fold_in(_tk, 500 + 6), (12500, 16), jnp.float32)
        tbl_7 = 0.05 * jax.random.normal(jax.random.fold_in(_tk, 500 + 7), (1250, 16), jnp.float32)
        tbl_8 = 0.05 * jax.random.normal(jax.random.fold_in(_tk, 500 + 8), (1250, 16), jnp.float32)
        tbl_9 = 0.05 * jax.random.normal(jax.random.fold_in(_tk, 500 + 9), (125000, 16), jnp.float32)
        tbl_10 = 0.05 * jax.random.normal(jax.random.fold_in(_tk, 500 + 10), (1000, 16), jnp.float32)
        tbl_11 = 0.05 * jax.random.normal(jax.random.fold_in(_tk, 500 + 11), (1000, 16), jnp.float32)
        tbl_12 = 0.05 * jax.random.normal(jax.random.fold_in(_tk, 500 + 12), (12500, 16), jnp.float32)
        tbl_13 = 0.05 * jax.random.normal(jax.random.fold_in(_tk, 500 + 13), (12500, 16), jnp.float32)
        tbl_14 = 0.05 * jax.random.normal(jax.random.fold_in(_tk, 500 + 14), (12500, 16), jnp.float32)
        tbl_15 = 0.05 * jax.random.normal(jax.random.fold_in(_tk, 500 + 15), (1000, 16), jnp.float32)
        tbl_16 = 0.05 * jax.random.normal(jax.random.fold_in(_tk, 500 + 16), (1250, 16), jnp.float32)
        tbl_17 = 0.05 * jax.random.normal(jax.random.fold_in(_tk, 500 + 17), (125000, 16), jnp.float32)
        tbl_18 = 0.05 * jax.random.normal(jax.random.fold_in(_tk, 500 + 18), (1000, 16), jnp.float32)
        tbl_19 = 0.05 * jax.random.normal(jax.random.fold_in(_tk, 500 + 19), (1000, 16), jnp.float32)
        tbl_20 = 0.05 * jax.random.normal(jax.random.fold_in(_tk, 500 + 20), (125000, 16), jnp.float32)
        tbl_21 = 0.05 * jax.random.normal(jax.random.fold_in(_tk, 500 + 21), (1000, 16), jnp.float32)
        tbl_22 = 0.05 * jax.random.normal(jax.random.fold_in(_tk, 500 + 22), (125000, 16), jnp.float32)
        tbl_23 = 0.05 * jax.random.normal(jax.random.fold_in(_tk, 500 + 23), (1000, 16), jnp.float32)
        tbl_24 = 0.05 * jax.random.normal(jax.random.fold_in(_tk, 500 + 24), (125000, 16), jnp.float32)
        tbl_25 = 0.05 * jax.random.normal(jax.random.fold_in(_tk, 500 + 25), (125000, 16), jnp.float32)
        tbl_26 = 0.05 * jax.random.normal(jax.random.fold_in(_tk, 500 + 26), (12500, 16), jnp.float32)
        tbl_27 = 0.05 * jax.random.normal(jax.random.fold_in(_tk, 500 + 27), (1000, 16), jnp.float32)
        tbl_28 = 0.05 * jax.random.normal(jax.random.fold_in(_tk, 500 + 28), (1000, 16), jnp.float32)
        tbl_29 = 0.05 * jax.random.normal(jax.random.fold_in(_tk, 500 + 29), (125000, 16), jnp.float32)
        tbl_30 = 0.05 * jax.random.normal(jax.random.fold_in(_tk, 500 + 30), (1000, 16), jnp.float32)
        tbl_31 = 0.05 * jax.random.normal(jax.random.fold_in(_tk, 500 + 31), (12500, 16), jnp.float32)
        tbl_32 = 0.05 * jax.random.normal(jax.random.fold_in(_tk, 500 + 32), (1250, 16), jnp.float32)
        tbl_33 = 0.05 * jax.random.normal(jax.random.fold_in(_tk, 500 + 33), (12500, 16), jnp.float32)
        tbl_34 = 0.05 * jax.random.normal(jax.random.fold_in(_tk, 500 + 34), (125000, 16), jnp.float32)
        tbl_35 = 0.05 * jax.random.normal(jax.random.fold_in(_tk, 500 + 35), (12500, 16), jnp.float32)
        tbl_36 = 0.05 * jax.random.normal(jax.random.fold_in(_tk, 500 + 36), (12500, 16), jnp.float32)
        tbl_37 = 0.05 * jax.random.normal(jax.random.fold_in(_tk, 500 + 37), (125000, 16), jnp.float32)
        tbl_38 = 0.05 * jax.random.normal(jax.random.fold_in(_tk, 500 + 38), (125000, 16), jnp.float32)
        _rk = jax.random.fold_in(_tk, 7)
        W_top1 = 0.0606339 * jax.random.normal(jax.random.fold_in(_tk, 801), (272, 512), jnp.float32)
        W_top2 = 0.0441942 * jax.random.normal(jax.random.fold_in(_tk, 802), (512, 256), jnp.float32)
        W_top3 = 0.0625 * jax.random.normal(jax.random.fold_in(_tk, 803), (256, 1), jnp.float32)
        b_top1 = jnp.zeros((512,), jnp.float32)
        b_top2 = jnp.zeros((256,), jnp.float32)
        return (dense_ctx, ids, tbl_0, tbl_1, tbl_2, tbl_3, tbl_4, tbl_5, tbl_6, tbl_7, tbl_8, tbl_9, tbl_10, tbl_11, tbl_12, tbl_13, tbl_14, tbl_15, tbl_16, tbl_17, tbl_18, tbl_19, tbl_20, tbl_21, tbl_22, tbl_23, tbl_24, tbl_25, tbl_26, tbl_27, tbl_28, tbl_29, tbl_30, tbl_31, tbl_32, tbl_33, tbl_34, tbl_35, tbl_36, tbl_37, tbl_38, W_top1, b_top1, W_top2, b_top2, W_top3)
    dense_ctx, ids, tbl_0, tbl_1, tbl_2, tbl_3, tbl_4, tbl_5, tbl_6, tbl_7, tbl_8, tbl_9, tbl_10, tbl_11, tbl_12, tbl_13, tbl_14, tbl_15, tbl_16, tbl_17, tbl_18, tbl_19, tbl_20, tbl_21, tbl_22, tbl_23, tbl_24, tbl_25, tbl_26, tbl_27, tbl_28, tbl_29, tbl_30, tbl_31, tbl_32, tbl_33, tbl_34, tbl_35, tbl_36, tbl_37, tbl_38, W_top1, b_top1, W_top2, b_top2, W_top3 = _rec_inputs()

    def _L0_rec_setup():
        import jax, jax.numpy as jnp
        import numpy as np
        B, F0, D = (256, 39, 16)
        LAYER_SIZES = [128, 128, 128]
        key = jax.random.key(seed)
        ks = jax.random.split(key, 1 + 2 * len(LAYER_SIZES))
        inputs = jax.random.normal(ks[0], (B, F0, D), dtype=jnp.float32)
        out = {'inputs': inputs}
        field_nums = [F0]
        for i, size in enumerate(LAYER_SIZES):
            fk = field_nums[-1]
            fan_in = F0 * fk
            scale = np.sqrt(2.0 / (fan_in + size)).astype(np.float32)
            out[f'w{i}'] = jax.random.normal(ks[1 + 2 * i], (F0, fk, size), dtype=jnp.float32) * scale
            out[f'b{i}'] = jnp.zeros((size,), dtype=jnp.float32)
            field_nums.append(size // 2)
        return out
    _L0_rec_all = _L0_rec_setup()
    _L0_rec_in = {k: v for k, v in _L0_rec_all.items() if k in ('w0', 'w1', 'w2', 'b0', 'b1', 'b2')}
    del _L0_rec_all
    return {'dense_ctx': dense_ctx, 'ids': ids, 'tbl_0': tbl_0, 'tbl_1': tbl_1, 'tbl_2': tbl_2, 'tbl_3': tbl_3, 'tbl_4': tbl_4, 'tbl_5': tbl_5, 'tbl_6': tbl_6, 'tbl_7': tbl_7, 'tbl_8': tbl_8, 'tbl_9': tbl_9, 'tbl_10': tbl_10, 'tbl_11': tbl_11, 'tbl_12': tbl_12, 'tbl_13': tbl_13, 'tbl_14': tbl_14, 'tbl_15': tbl_15, 'tbl_16': tbl_16, 'tbl_17': tbl_17, 'tbl_18': tbl_18, 'tbl_19': tbl_19, 'tbl_20': tbl_20, 'tbl_21': tbl_21, 'tbl_22': tbl_22, 'tbl_23': tbl_23, 'tbl_24': tbl_24, 'tbl_25': tbl_25, 'tbl_26': tbl_26, 'tbl_27': tbl_27, 'tbl_28': tbl_28, 'tbl_29': tbl_29, 'tbl_30': tbl_30, 'tbl_31': tbl_31, 'tbl_32': tbl_32, 'tbl_33': tbl_33, 'tbl_34': tbl_34, 'tbl_35': tbl_35, 'tbl_36': tbl_36, 'tbl_37': tbl_37, 'tbl_38': tbl_38, 'W_top1': W_top1, 'b_top1': b_top1, 'W_top2': W_top2, 'b_top2': b_top2, 'W_top3': W_top3, 'L0_rec_w0': _L0_rec_in['w0'], 'L0_rec_w1': _L0_rec_in['w1'], 'L0_rec_w2': _L0_rec_in['w2'], 'L0_rec_b0': _L0_rec_in['b0'], 'L0_rec_b1': _L0_rec_in['b1'], 'L0_rec_b2': _L0_rec_in['b2']}

def reference(dense_ctx, ids, tbl_0, tbl_1, tbl_2, tbl_3, tbl_4, tbl_5, tbl_6, tbl_7, tbl_8, tbl_9, tbl_10, tbl_11, tbl_12, tbl_13, tbl_14, tbl_15, tbl_16, tbl_17, tbl_18, tbl_19, tbl_20, tbl_21, tbl_22, tbl_23, tbl_24, tbl_25, tbl_26, tbl_27, tbl_28, tbl_29, tbl_30, tbl_31, tbl_32, tbl_33, tbl_34, tbl_35, tbl_36, tbl_37, tbl_38, W_top1, b_top1, W_top2, b_top2, W_top3, L0_rec_w0, L0_rec_w1, L0_rec_w2, L0_rec_b0, L0_rec_b1, L0_rec_b2):
    import jax
    import jax.numpy as jnp

    def _L0_rec_ref(inputs, w0, w1, w2, b0, b1, b2):
        import jax, jax.numpy as jnp
        import numpy as np
        B, F0, D = (256, 39, 16)
        LAYER_SIZES = [128, 128, 128]
        x0 = inputs
        xk = inputs
        params = [(w0, b0), (w1, b1), (w2, b2)]
        n_layers = len(params)
        direct = []
        for idx, (W, b) in enumerate(params):
            z = jnp.einsum('bhd,bkd,hks->bsd', x0, xk, W) + b[None, :, None]
            z = jax.nn.relu(z)
            if idx != n_layers - 1:
                half = z.shape[1] // 2
                xk = z[:, :half, :]
                direct.append(z[:, half:, :])
            else:
                direct.append(z)
        logit = jnp.sum(jnp.concatenate(direct, axis=1), axis=-1)
        return logit
    e = jnp.stack([tbl_0[ids[:, 0]], tbl_1[ids[:, 1]], tbl_2[ids[:, 2]], tbl_3[ids[:, 3]], tbl_4[ids[:, 4]], tbl_5[ids[:, 5]], tbl_6[ids[:, 6]], tbl_7[ids[:, 7]], tbl_8[ids[:, 8]], tbl_9[ids[:, 9]], tbl_10[ids[:, 10]], tbl_11[ids[:, 11]], tbl_12[ids[:, 12]], tbl_13[ids[:, 13]], tbl_14[ids[:, 14]], tbl_15[ids[:, 15]], tbl_16[ids[:, 16]], tbl_17[ids[:, 17]], tbl_18[ids[:, 18]], tbl_19[ids[:, 19]], tbl_20[ids[:, 20]], tbl_21[ids[:, 21]], tbl_22[ids[:, 22]], tbl_23[ids[:, 23]], tbl_24[ids[:, 24]], tbl_25[ids[:, 25]], tbl_26[ids[:, 26]], tbl_27[ids[:, 27]], tbl_28[ids[:, 28]], tbl_29[ids[:, 29]], tbl_30[ids[:, 30]], tbl_31[ids[:, 31]], tbl_32[ids[:, 32]], tbl_33[ids[:, 33]], tbl_34[ids[:, 34]], tbl_35[ids[:, 35]], tbl_36[ids[:, 36]], tbl_37[ids[:, 37]], tbl_38[ids[:, 38]]], axis=1)
    z = _L0_rec_ref(e, L0_rec_w0, L0_rec_w1, L0_rec_w2, L0_rec_b0, L0_rec_b1, L0_rec_b2)
    z = z.reshape(z.shape[0], -1)
    h = jnp.concatenate([z, dense_ctx], axis=1)
    h = jnp.maximum(h @ W_top1 + b_top1, 0.0)
    h = jnp.maximum(h @ W_top2 + b_top2, 0.0)
    y = h @ W_top3
    return y

_drawn_inputs = setup_inputs


def setup_inputs(seed=0):
    import zlib

    import numpy as np

    out = dict(_drawn_inputs(seed))
    spreads = {'b_top1': (0.0, 2.0),
     'b_top2': (0.0, 2.0),
     'L0_rec_b0': (0.0, 0.353),
     'L0_rec_b1': (0.0, 0.532),
     'L0_rec_b2': (0.0, 0.8)}
    factors = {'tbl_0': 8.0,
     'tbl_1': 8.0,
     'tbl_2': 8.0,
     'tbl_3': 8.0,
     'tbl_4': 8.0,
     'tbl_5': 8.0,
     'tbl_6': 8.0,
     'tbl_7': 8.0,
     'tbl_8': 8.0,
     'tbl_9': 8.0,
     'tbl_10': 8.0,
     'tbl_11': 8.0,
     'tbl_12': 8.0,
     'tbl_13': 8.0,
     'tbl_14': 8.0,
     'tbl_15': 8.0,
     'tbl_16': 8.0,
     'tbl_17': 8.0,
     'tbl_18': 8.0,
     'tbl_19': 8.0,
     'tbl_20': 8.0,
     'tbl_21': 8.0,
     'tbl_22': 8.0,
     'tbl_23': 8.0,
     'tbl_24': 8.0,
     'tbl_25': 8.0,
     'tbl_26': 8.0,
     'tbl_27': 8.0,
     'tbl_28': 8.0,
     'tbl_29': 8.0,
     'tbl_30': 8.0,
     'tbl_31': 8.0,
     'tbl_32': 8.0,
     'tbl_33': 8.0,
     'tbl_34': 8.0,
     'tbl_35': 8.0,
     'tbl_36': 8.0,
     'tbl_37': 8.0,
     'tbl_38': 8.0,
     'L0_rec_w0': 8.0,
     'L0_rec_w1': 6.25,
     'L0_rec_w2': 4.829,
     'dense_ctx': 8.0}
    for name, (base, spread) in spreads.items():
        noise = np.random.default_rng([zlib.crc32(name.encode()), seed]).standard_normal(out[name].shape)
        drawn = base * np.exp(spread * noise) if base else spread * noise
        out[name] = jnp.asarray(drawn.astype(out[name].dtype))
    for name, factor in factors.items():
        out[name] = (out[name] * factor).astype(out[name].dtype)
    return out
```

```python
import concourse.bass as bass
from concourse import mybir

FP32 = mybir.dt.float32
FP32R = mybir.dt.float32r
I32 = mybir.dt.int32
ALU = mybir.AluOpType
ACT = mybir.ActivationFunctionType
AX = mybir.AxisListType

B, F, D, S = 1024, 39, 16, 128
HALF = S // 2
CHUNK = 128
CHUNKS = B // CHUNK
QS = 4
SB = CHUNK // QS
N = SB * D
STEPS = CHUNKS * QS
SHIFTS = (F + 1) // 2
SLOTS = S // F
ROWS0 = SLOTS * F
TILES0 = -(-SHIFTS // SLOTS)
LAST0 = (SHIFTS - SLOTS * (TILES0 - 1)) * F
TILES = (F + 1) // 2
LASTT = (F - 2 * (TILES - 1)) * HALF
GT = 2
GROUPS = [(a, a + GT) for a in (*range(0, TILES - 2 * GT, GT), TILES - GT, TILES - 2 * GT)]
NG = len(GROUPS)
TAIL = NG - 2
SPLIT = {1: (0, 2, 3, 5, 6, TAIL), 2: (2, 4, 5, 6, TAIL)}
TWICE = {1: (0, 2, 4, 6), 2: (2, 4, 6)}
POOL_GROUPS = [(0, 4), (4, TILES0)]
G_FIRST = 2 * NG
G_STEP = 2 * NG
K_FIRST = 2 * len(SPLIT[1])
K_STEP = len(SPLIT[1]) + len(SPLIT[2])
GATHERS = 20
PAIRS = (0, 6, 12, TILES)
RELU0_AFTER = 5
RELU2_AFTER = 4
TR_AT = 1
SUM2_AT = 9
SUM01_AT = 6
RING = 8
HRING = 4
J1, J2, DENSE = 512, 256, 16
MN = 512


def rows_of(layer, tile):
    if layer == 0:
        return LAST0 if tile == TILES0 - 1 else ROWS0
    return LASTT if tile == TILES - 1 else S


def is_split(layer, t):
    if layer == 0:
        return False
    g = next(g for g, (a, b) in enumerate(GROUPS) if a <= t < b)
    return g in SPLIT[layer] and (g != TAIL or t == TILES - 1)


def tile_at(layer, t):
    before = [(l, x) for l in range(3) for x in range(TILES if l else TILES0)]
    before = before[:before.index((layer, t))]
    return sum(is_split(*x) == is_split(layer, t) for x in before)


def build(nc, dense, ids, tables, wa, wb, w1, w2, biases, wt1, bt1, wt2, bt2, wt3, ident, out):
    def sb(name, shape, dt=FP32):
        return nc.alloc_sbuf_tensor(name, shape, dt)

    sem = nc.alloc_semaphore

    x0_dram = nc.dram_tensor("x0_scratch", [STEPS, 2 * F, N], FP32).ap()

    ids_all = sb("ids_all", [CHUNK, CHUNKS, F], I32)
    ids_now = sb("ids_now", [CHUNK, F], I32)
    emb = sb("emb", [CHUNK, F * D])
    x0t = sb("x0t", [F, QS, D, SB])
    eye = sb("eye", [128, 128])
    x0_rep = sb("x0_rep", [ROWS0, N])
    x0_shift = sb("x0_shift", [ROWS0, TILES0, N])
    x0_pair = sb("x0_pair", [S, 2, TILES, N])
    direct01 = sb("direct01", [S, 2, N])
    direct2 = sb("direct2", [S, N])
    logit01 = sb("logit01", [S, B])
    logit2 = sb("logit2", [S, B])
    prod_ptr = nc.sbuf_base
    prod = sb("prod", [S, RING, GT, N])
    low = nc.alloc_sbuf_tensor_at("low", [S, RING, GT, N], FP32R, offset=prod_ptr)
    high = sb("high", [S, HRING, GT, N], FP32R)
    kinds = [is_split(l, t) for l in range(3) for t in range(TILES if l else TILES0)]
    n32, nsp = kinds.count(False), kinds.count(True)
    w_32 = sb("w_32", [S, n32, S])
    w_hi = sb("w_hi", [S, nsp, S], FP32R)
    w_lo = sb("w_lo", [S, nsp, S], FP32R)
    bias = sb("bias", [S, 3])
    bias_t1 = sb("bias_t1", [128, J1 // 128])
    bias_t2 = sb("bias_t2", [128, J2 // 128])
    w_t3 = sb("w_t3", [128, J2 // 128])

    stage = prod[:, :, :, :].rearrange("p r g n -> p (r g n)").rearrange("p (t s) -> p t s", s=S)
    STAGE = {0: 0, 1: 2 * TILES0, 2: 2 * TILES0 + TILES}
    even = x0_pair[:, 0, :, :].rearrange("p t n -> p (t n)")
    odd = x0_pair[:, 1, :, :].rearrange("p t n -> p (t n)")
    w_t1 = even[:, 0:3 * J1].rearrange("p (k j) -> p k j", k=3)
    w_t2 = even[:, 3 * J1:3 * J1 + 4 * J2].rearrange("p (k j) -> p k j", k=4)
    dense_t = even[0:DENSE, 3 * J1 + 4 * J2:3 * J1 + 4 * J2 + B]
    y_row = even[0:1, 3 * J1 + 4 * J2 + B:3 * J1 + 4 * J2 + 2 * B]
    dense_in = even[:, 3 * J1 + 4 * J2 + 2 * B:3 * J1 + 4 * J2 + 2 * B + CHUNKS * DENSE].rearrange(
        "p (c f) -> p c f", f=DENSE)
    h1 = odd[:, 0:4 * B].rearrange("p (m b) -> p m b", m=4)
    h2 = odd[:, 4 * B:6 * B].rearrange("p (m b) -> p m b", m=2)

    z_ps = {l: nc.alloc_psum_tensor(f"z{l}_ps", [S, N], FP32) for l in range(3)}
    tr_ps = [nc.alloc_psum_tensor(f"tr{i}_ps", [S, N], FP32) for i in range(2)]
    x_dup = {l: nc.alloc_psum_tensor(f"x{l}_dup", [S, N], FP32) for l in (1, 2)}
    mlp_ps = list(z_ps.values())
    MR = len(mlp_ps)

    s_ids, s_idsc, s_eye, s_dense = sem("ids_loaded"), sem("ids_copied"), sem("eye_loaded"), sem("dense_loaded")
    s_w, s_bias, s_wz = sem("weights_loaded"), sem("biases_loaded"), sem("weights_zeroed")
    s_xz = sem("x0_pads_zeroed")
    s_ws, s_wp = sem("weights_summed"), sem("weights_ready")
    s_emb = sem("emb_gathered")
    s_tr, s_trc, s_scr = sem("transposed"), sem("transposes_copied"), sem("x0_stored")
    s_shift = sem("shifts_loaded")
    s_pair = [[sem(f"pairs_loaded_{p}_{part}") for part in range(len(PAIRS) - 1)] for p in ("even", "odd")]
    s_prod0, s_used0 = sem("layer0_products_ready"), sem("layer0_products_used")
    s_prod, s_used = sem("products_ready"), sem("products_used")
    s_hi, s_lo = sem("high_ready"), sem("low_ready")
    s_z = {l: sem(f"z{l}_ready") for l in range(3)}
    s_x = {1: sem("x1_ready"), 2: sem("x2_ready")}
    s_d = {l: sem(f"direct{l}_ready") for l in range(3)}
    s_sum01, s_sum2 = sem("direct01_summed"), sem("direct2_summed")
    s_wt = sem("mlp_weights_loaded")
    s_dtr, s_dtc = sem("dense_transposed"), sem("dense_copied")
    s_m, s_mr = sem("mlp_product_ready"), sem("mlp_relu_done")
    s_out = sem("y_stored")
    s_pe_note, s_pool_note = sem("transposes_begun"), sem("gathers_begun")
    s_sp_note = sem("chunk_loads_begun")

    def layers_of(c, q):
        if c is None:
            return (0, 1)
        return (2,) if q >= QS - 2 and isinstance(c, int) and c == CHUNKS - 1 else (0, 2, 1)

    def start_of(c, q, layer):
        if c is None:
            return NG * q, len(SPLIT[1]) * q
        g, k = G_FIRST + G_STEP * q + G_STEP * QS * c, K_FIRST + K_STEP * q + K_STEP * QS * c
        if isinstance(c, int) and c == CHUNKS - 1 and q == QS - 1:
            return g - NG, k - len(SPLIT[1])
        return (g, k) if layer in (0, 2) else (g + NG, k + len(SPLIT[2]))

    def step_of(c, q, layer):
        return q if c is None else QS * c + (q + (0 if layer == 2 else 2))

    def slot_of(c, q, layer):
        return start_of(c if c is None or layers_of(c, q) == (2,) else 0, q, layer)

    block = nc.Block()
    with block:

        @block.sync
        def _(sp):
            sp.dma_start(ids_all[:, :, :], ids.rearrange("(c p) f -> p c f", p=CHUNK)).then_inc(s_ids, 16)
            sp.dma_start(eye[:, :], ident).then_inc(s_eye, 16)
            sp.wait_ge(s_wz, 1)
            full = ROWS0 * (TILES0 - 1)
            sp.dma_start(stage[0:ROWS0, 0:TILES0 - 1, :],
                         wa[0:full, :].rearrange("(t p) s -> p t s", p=ROWS0)).then_inc(s_w, 16)
            sp.dma_start(stage[0:LAST0, TILES0 - 1, :], wa[full:full + LAST0, :]).then_inc(s_w, 16)
            sp.dma_start(stage[F:ROWS0, TILES0, :], wb[F:ROWS0, :]).then_inc(s_w, 16)
            sp.dma_start(stage[0:ROWS0, TILES0 + 1:2 * TILES0 - 1, :],
                         wb[ROWS0:full, :].rearrange("(t p) s -> p t s", p=ROWS0)).then_inc(s_w, 16)
            sp.dma_start(stage[0:LAST0, 2 * TILES0 - 1, :], wb[full:full + LAST0, :]).then_inc(s_w, 16)
            for l, w in ((1, w1), (2, w2)):
                flat = w.rearrange("h k s -> (h k) s")
                n = S * (TILES - 1)
                sp.dma_start(stage[:, STAGE[l]:STAGE[l] + TILES - 1, :],
                             flat[0:n, :].rearrange("(t p) s -> p t s", p=S)).then_inc(s_w, 16)
                sp.dma_start(stage[0:LASTT, STAGE[l] + TILES - 1, :], flat[n:n + LASTT, :]).then_inc(s_w, 16)

            def row(i, r):
                return x0_dram[i, r, :]

            def load_shifts(i):
                for j in range(SLOTS):
                    tiles = len(range(j, SHIFTS, SLOTS))
                    at = row(i, j)
                    sp.dma_start(x0_shift[j * F:(j + 1) * F, 0:tiles, :],
                                 bass.AP(at.tensor, at.offset, [[N, F], [SLOTS * N, tiles], [1, N]])).then_inc(s_shift, 16)
                    sp.dma_start(x0_rep[j * F:(j + 1) * F, :], x0_dram[i, 0:F, :]).then_inc(s_shift, 16)

            def load_pairs(i, parity):
                for part, (t0, t1) in enumerate(zip(PAIRS, PAIRS[1:])):
                    if not (isinstance(i, int) and i < 2):
                        sp.wait_ge(s_prod, G_STEP * i + (G_FIRST - 2 * G_STEP + (NG if t1 == TILES else t1 // GT)))
                    for j in range(2):
                        tiles = len(range(2 * t0 + j, min(2 * t1, F), 2))
                        at = row(i, 2 * t0 + j)
                        sp.dma_start(x0_pair[j * HALF:(j + 1) * HALF, parity, t0:t0 + tiles, :],
                                     bass.AP(at.tensor, at.offset, [[0, HALF], [2 * N, tiles], [1, N]])
                                     ).then_inc(s_pair[parity][part], 16)

            def chunk(c):
                sp.wait_ge(s_scr, 32 * (c + 1))
                sp.sem_inc(s_sp_note, 1)
                for q in range(QS):
                    i = QS * c + q
                    if not (isinstance(c, int) and i == 0):
                        sp.wait_ge(s_used0, i)
                    load_shifts(i)
                    load_pairs(i, q % 2)

            sp.wait_ge(s_xz, 1)
            chunk(0)
            with sp.Fori(1, CHUNKS) as c:
                chunk(c)

            sp.wait_ge(s_prod, start_of(CHUNKS - 1, QS - 2, 2)[0] + NG)
            sp.dma_start(dense_in, dense.rearrange("(c p) f -> p c f", p=CHUNK)).then_inc(s_dense, 16)
            sp.dma_start(w_t1[:, 0:2, :], wt1[0:2 * S, :].rearrange("(k p) j -> p k j", p=S)).then_inc(s_wt, 16)
            sp.dma_start(w_t1[0:DENSE, 2, :], wt1[2 * S:2 * S + DENSE, :]).then_inc(s_wt, 16)
            sp.dma_start(w_t2, wt2.rearrange("(k p) j -> p k j", p=128)).then_inc(s_wt, 16)
            sp.wait_ge(s_mr, 2 * 4 + 2 * 2 + 2)
            sp.dma_start(out.rearrange("b o -> o b"), y_row[:, :]).then_inc(s_out, 16)
            sp.wait_ge(s_out, 16)

        @block.gpsimd
        def _(pool):
            pool.wait_ge(s_ids, 16)

            def indices(c):
                nc.gpsimd.tensor_copy(ids_now[:, :], ids_all[:, c, :]).then_inc(s_idsc, 1)
                pool.wait_ge(s_idsc, c + 1)
                pool.sem_inc(s_pool_note, 1)

            def gather(f0, f1):
                for f in range(f0, f1):
                    pool.indirect_dma_start(emb[:, f * D:(f + 1) * D], None, tables[f][:, :],
                                            bass.IndirectOffsetOnAxis(ap=ids_now[:, f:f + 1], axis=0)).then_inc(s_emb, 16)

            def store(c):
                pool.wait_ge(s_trc, QS * (c + 1))
                for half in range(2):
                    dst = x0_dram[bass.ds(QS * c, QS), half * F:(half + 1) * F, :]
                    pool.dma_start(dst.rearrange("q f n -> f q n"),
                                   x0t[:, :, :, :].rearrange("f q d b -> f q (d b)")).then_inc(s_scr, 16)

            def products0(step):
                pool.wait_ge(s_shift, 2 * SLOTS * 16 * (step + 1))
                for a, b in POOL_GROUPS:
                    nc.gpsimd.tensor_tensor(x0_shift[:, a:b, :], x0_shift[:, a:b, :],
                                            x0_rep[:, :].unsqueeze(1).to_broadcast([ROWS0, b - a, N]),
                                            ALU.mult).then_inc(s_prod0, 1)

            indices(0)
            gather(0, F)
            store(0)
            products0(0)
            products0(1)
            with pool.Fori(0, CHUNKS - 1) as c:
                pool.wait_ge(s_tr, QS * (c + 1))
                pool.wait_ge(s_emb, 16 * F * (c + 1))
                indices(c + 1)
                gather(0, GATHERS)
                products0(QS * c + 2)
                gather(GATHERS, F)
                products0(QS * c + 3)
                store(c + 1)
                products0(QS * c + 4)
                products0(QS * c + 5)
            for q in range(2, QS):
                products0(QS * (CHUNKS - 1) + q)

        @block.tensor
        def _(pe):
            def transposes(c):
                pe.wait_ge(s_emb, 16 * F * (c + 1))
                rows = emb[:, :].rearrange("b (f d) -> b d f", d=D)
                for r in range(4):
                    if not (isinstance(c, int) and c == 0 and r < 2):
                        pe.wait_ge(s_trc, 4 * c + r - 1)
                    pe.sem_inc(s_pe_note, 1)
                    for d in range(4):
                        last = nc.tensor.transpose(tr_ps[r % 2][0:F, d * CHUNK:(d + 1) * CHUNK],
                                                   rows[:, 4 * r + d, :], eye[:, :])
                    last.then_inc(s_tr, 1)

            def layer(l, c, q, step):
                g0, k0 = start_of(c, q, l)
                sg, sk = slot_of(c, q, l)
                if l == 2:
                    pe.wait_ge(s_d[l], step + 1)
                elif not (isinstance(step, int) and step == 0):
                    pe.wait_ge(s_d[l], step)
                if l == 0:
                    for g, (a, b) in enumerate(POOL_GROUPS):
                        pe.wait_ge(s_prod0, len(POOL_GROUPS) * step + g + 1)
                        for t in range(a, b):
                            n = rows_of(l, t)
                            last = nc.tensor.matmul(z_ps[l][:, :], w_32[0:n, tile_at(l, t), :], x0_shift[0:n, t, :],
                                                    start=(t == 0), stop=(t == TILES0 - 1))
                    last.then_inc(s_used0, 1)
                    return
                k = 0
                left = sum((3 if rows_of(l, t) > HALF else 2) if is_split(l, t) else 1
                           for t in range(TILES))
                first = [True]

                def product(w, p):
                    nonlocal left
                    left -= 1
                    last = nc.tensor.matmul(z_ps[l][:, :], w, p, start=first[0], stop=(left == 0))
                    first[0] = False
                    return last

                for g, (a, b) in enumerate(GROUPS):
                    slot = (sg + g) % RING
                    if g in SPLIT[l]:
                        hslot = (sk + k) % HRING
                        if g == TAIL:
                            pe.wait_ge(s_prod, g0 + g + 1)
                            for t in range(a, b - 1):
                                product(w_32[0:rows_of(l, t), tile_at(l, t), :], prod[0:rows_of(l, t), slot, t - a, :])
                            at = tile_at(l, b - 1)
                            pe.wait_ge(s_hi, k0 + k + 1)
                            product(w_lo[0:LASTT, at, :], high[0:LASTT, hslot, 0, :])
                            pe.wait_ge(s_lo, k0 + k + 1)
                            last = product(w_hi[:, at, :], high[:, hslot, 0, :])
                        else:
                            pe.wait_ge(s_hi, k0 + k + 1)
                            for t in range(a, b):
                                n, at = rows_of(l, t), tile_at(l, t)
                                product(w_hi[0:n, at, :], high[0:n, hslot, t - a, :])
                                product(w_lo[0:n, at, :], high[0:n, hslot, t - a, :])
                            pe.wait_ge(s_lo, k0 + k + 1)
                            for t in range(a, b):
                                n, at = rows_of(l, t), tile_at(l, t)
                                last = product(w_hi[0:n, at, :], low[0:n, slot, t - a, :])
                        k += 1
                    else:
                        pe.wait_ge(s_prod, g0 + g + 1)
                        for t in range(a, b):
                            n, at = rows_of(l, t), tile_at(l, t)
                            last = product(w_32[0:n, at, :], prod[0:n, slot, t - a, :])
                    last.then_inc(s_used, 1)

            pe.wait_ge(s_eye, 16)
            transposes(0)
            pe.wait_ge(s_wp, 1)
            for step in range(2):
                layer(0, None, step, step)
                layer(1, None, step, step)

            def body(c, q):
                for l in layers_of(c, q):
                    layer(l, c, q, step_of(c, q, l))
                    if l == 0 and q == TR_AT and not (isinstance(c, int) and c == CHUNKS - 1):
                        transposes(c + 1)

            with pe.Fori(0, CHUNKS - 1) as c:
                for q in range(QS):
                    body(c, q)
            for q in range(QS):
                body(CHUNKS - 1, q)

            pe.wait_ge(s_dense, 16)
            for r in range(2):
                for j in range(4):
                    last = nc.tensor.transpose(tr_ps[r][0:DENSE, j * CHUNK:(j + 1) * CHUNK],
                                               dense_in[:, 4 * r + j, :], eye[:, :])
                last.then_inc(s_dtr, 1)
            pe.wait_ge(s_wt, 48)
            pe.wait_ge(s_d[2], STEPS + 1)
            pe.wait_ge(s_dtc, 2)
            pe.wait_ge(s_sum01, STEPS + 2)
            pe.wait_ge(s_sum2, STEPS + 1)
            n = 0
            for nb in range(B // MN):
                cols = slice(nb * MN, (nb + 1) * MN)
                for m in range(J1 // 128):
                    if n >= MR:
                        pe.wait_ge(s_mr, n - MR + 1)
                    ps = mlp_ps[n % MR]
                    js = slice(m * 128, (m + 1) * 128)
                    nc.tensor.matmul(ps[:, :], w_t1[:, 0, js], logit01[:, cols], start=True, stop=False)
                    nc.tensor.matmul(ps[:, :], w_t1[:, 1, js], logit2[:, cols], start=False, stop=False)
                    nc.tensor.matmul(ps[:, :], w_t1[0:DENSE, 2, js], dense_t[:, cols],
                                     start=False, stop=True).then_inc(s_m, 1)
                    n += 1
            for nb in range(B // MN):
                cols = slice(nb * MN, (nb + 1) * MN)
                pe.wait_ge(s_mr, 4 * (nb + 1))
                for m in range(J2 // 128):
                    pe.wait_ge(s_mr, n - MR + 1)
                    js = slice(m * 128, (m + 1) * 128)
                    for k in range(4):
                        last = nc.tensor.matmul(mlp_ps[n % MR][:, :], w_t2[:, k, js], h1[:, k, cols],
                                                start=(k == 0), stop=(k == 3))
                    last.then_inc(s_m, 1)
                    n += 1
            for nb in range(B // MN):
                cols = slice(nb * MN, (nb + 1) * MN)
                pe.wait_ge(s_mr, 8 + 2 * (nb + 1))
                pe.wait_ge(s_mr, n - MR + 1)
                for k in range(2):
                    last = nc.tensor.matmul(mlp_ps[n % MR][0:1, :], w_t3[:, k:k + 1], h2[:, k, cols],
                                            start=(k == 0), stop=(k == 1))
                last.then_inc(s_m, 1)
                n += 1

        @block.scalar
        def _(act):
            with nc.allow_non_contiguous_dma("one column of biases"):
                for l in range(3):
                    act.dma_start(bias[:, l:l + 1], biases[l].unsqueeze(1)).then_inc(s_bias, 16)
                act.dma_start(bias_t1[:, :], bt1.rearrange("(m p) -> p m", p=128)).then_inc(s_bias, 16)
                act.dma_start(bias_t2[:, :], bt2.rearrange("(m p) -> p m", p=128)).then_inc(s_bias, 16)
                act.dma_start(w_t3[:, :], wt3.rearrange("(m p) o -> p (m o)", p=128)).then_inc(s_bias, 16)

            def copy_transposes(c):
                if not (isinstance(c, int) and c == 0):
                    act.wait_ge(s_scr, 32 * c)
                for r in range(4):
                    act.wait_ge(s_tr, 4 * c + r + 1)
                    nc.scalar.copy(x0t[:, :, 4 * r:4 * r + 4, :],
                                   tr_ps[r % 2][0:F, :].rearrange("f (d q b) -> f q d b", d=4, q=QS)).then_inc(s_trc, 1)

            def round_high(l, g, c, q):
                g0, k0 = start_of(c, q, l)
                sg, sk = slot_of(c, q, l)
                k = SPLIT[l].index(g)
                a, b = GROUPS[g]
                n = S
                act.wait_ge(s_prod, g0 + g + 1)
                if not (c is None and sk + k < HRING):
                    act.wait_ge(s_used, g0 + g - groups_back(c, q, l, g, HRING) + 1)
                if g == TAIL:
                    nc.scalar.copy(high[0:LASTT, (sk + k) % HRING, 0, :],
                                   prod[0:LASTT, (sg + g) % RING, b - 1 - a, :]).then_inc(s_hi, 1)
                else:
                    nc.scalar.copy(high[0:n, (sk + k) % HRING, 0:b - a, :],
                                   prod[0:n, (sg + g) % RING, 0:b - a, :]).then_inc(s_hi, 1)

            def groups_back(c, q, l, g, back):
                before = (1,) * q if c is None else (1, 2) if q == QS - 1 and layers_of(c, q) == (2,) else (1,)
                order = [(y, x) for y in before + layers_of(c, q) if y for x in range(NG)]
                here = at = max(n for n, x in enumerate(order) if x == (l, g))
                while back:
                    at -= 1
                    back -= order[at][1] in SPLIT[order[at][0]]
                assert at >= 0
                return here - at

            def relus(l, step, parity, groups=None):
                if l == 0:
                    act.wait_ge(s_used0, step + 1)
                else:
                    act.wait_ge(s_used, groups)
                first = isinstance(step, int) and step == 0
                if l < 2:
                    if not first:
                        act.wait_ge(s_prod, NG if l == 0 and isinstance(step, int) and step == 1
                                    else G_STEP * step + (G_FIRST + (-2 * G_STEP if l == 0 else NG - G_STEP)))
                    nc.scalar.activation(x_dup[l + 1][0:HALF, :], z_ps[l][0:HALF, :], ACT.Relu, bias=bias[0:HALF, l:l + 1])
                    nc.scalar.activation(x_dup[l + 1][HALF:S, :], z_ps[l][0:HALF, :], ACT.Relu,
                                         bias=bias[0:HALF, l:l + 1]).then_inc(s_x[l + 1], 1)
                    act.wait_ge(s_sum01, step + 1)
                    nc.scalar.activation(direct01[l * HALF:(l + 1) * HALF, parity, :], z_ps[l][HALF:S, :], ACT.Relu,
                                         bias=bias[HALF:S, l:l + 1]).then_inc(s_d[l], 1)
                else:
                    act.wait_ge(s_sum2, step + 1)
                    nc.scalar.activation(direct2[:, :], z_ps[l][:, :], ACT.Relu, bias=bias[:, l:l + 1]).then_inc(s_d[l], 1)

            act.wait_ge(s_bias, 96)
            copy_transposes(0)
            relus(0, 0, 0)
            for g in SPLIT[1]:
                round_high(1, g, None, 0)
            relus(1, 0, 0, NG)
            relus(0, 1, 1)
            for g in SPLIT[1]:
                round_high(1, g, None, 1)

            def body(c, q):
                start = start_of(c, q, 2)[0]
                layers = layers_of(c, q)
                for g in range(NG):
                    if g == RELU0_AFTER and 0 in layers:
                        relus(0, QS * c + (q + 2), q % 2)
                        if q == TR_AT and not (isinstance(c, int) and c == CHUNKS - 1):
                            copy_transposes(c + 1)
                    if g in SPLIT[2]:
                        round_high(2, g, c, q)
                if 1 in layers or q == QS - 2:
                    relus(1, QS * c + (q + 1), (q + 1) % 2, start)
                for g in range(NG if 1 in layers else 0):
                    if g == RELU2_AFTER:
                        relus(2, QS * c + q, q % 2, start + NG)
                    if g in SPLIT[1]:
                        round_high(1, g, c, q)
                if 1 not in layers:
                    relus(2, QS * c + q, q % 2, start + NG)

            with act.Fori(0, CHUNKS - 1) as c:
                for q in range(QS):
                    body(c, q)
            for q in range(QS):
                body(CHUNKS - 1, q)

            act.wait_ge(s_prod, start_of(CHUNKS - 1, QS - 2, 2)[0] + NG)
            for r in range(2):
                act.wait_ge(s_dtr, r + 1)
                nc.scalar.copy(dense_t[:, r * MN:(r + 1) * MN], tr_ps[r][0:DENSE, :]).then_inc(s_dtc, 1)
            n = 0
            for dst, b_col, m_tiles in ((h1, bias_t1, 4), (h2, bias_t2, 2)):
                for nb in range(B // MN):
                    for m in range(m_tiles):
                        act.wait_ge(s_m, n + 1)
                        nc.scalar.activation(dst[:, m, nb * MN:(nb + 1) * MN], mlp_ps[n % MR][:, :], ACT.Relu,
                                             bias=b_col[:, m:m + 1]).then_inc(s_mr, 1)
                        n += 1
            for nb in range(B // MN):
                act.wait_ge(s_m, n + 1)
                nc.scalar.copy(y_row[:, nb * MN:(nb + 1) * MN], mlp_ps[n % MR][0:1, :]).then_inc(s_mr, 1)
                n += 1

        @block.vector
        def _(dve):
            for t in (TILES0 - 1, TILES0):
                nc.vector.memset(stage[:, t, :], 0.0)
            nc.vector.memset(stage[:, 2 * TILES0 - 1, :], 0.0).then_inc(s_sum2, 1)
            nc.vector.memset(stage[:, STAGE[1] + TILES - 1, :], 0.0).then_inc(s_d[2], 1)
            nc.vector.memset(stage[:, STAGE[2] + TILES - 1, :], 0.0).then_inc(s_wz, 1)
            nc.vector.memset(x0_shift[:, TILES0 - 1, :], 0.0).then_inc(s_sum01, 2)
            nc.vector.memset(x0_pair[HALF:S, :, TILES - 1, :], 0.0).then_inc(s_xz, 1)
            dve.wait_ge(s_w, 9 * 16)
            nc.vector.tensor_tensor(stage[0:ROWS0, 0:TILES0, :], stage[0:ROWS0, 0:TILES0, :],
                                    stage[0:ROWS0, TILES0:2 * TILES0, :], ALU.add).then_inc(s_ws, 1)
            dve.wait_ge(s_ws, 1)

            def weights_of(split):
                for l in range(3):
                    n = ROWS0 if l == 0 else S
                    for t in range(TILES if l else TILES0):
                        if is_split(l, t) == split:
                            yield stage[0:n, STAGE[l] + t, :], (slice(0, n), tile_at(l, t))

            for raw, at in weights_of(False):
                nc.vector.tensor_copy(w_32[at], raw)
            for raw, at in weights_of(True):
                last = nc.vector.tensor_copy(w_hi[at], raw)
            last.then_inc(s_ws, 1)
            dve.wait_ge(s_ws, 2)
            for raw, at in weights_of(True):
                last = nc.vector.tensor_tensor(w_lo[at], raw, w_hi[at].bitcast(FP32), ALU.subtract)
            last.then_inc(s_ws, 1)
            dve.wait_ge(s_ws, 3)
            for l in (1, 2):
                at = tile_at(l, TILES - 1)
                last = nc.vector.tensor_copy(w_hi[HALF:S, at, :], w_hi[0:HALF, at, :])
            last.then_inc(s_wp, 1)
            dve.wait_ge(s_wp, 1)

            ring = prod[:, :, :, :].rearrange("p r g n -> p (r g) n")

            def products(l, g, groups, c, q, step, parity):
                g0, _ = start_of(c, q, l)
                sg, _ = slot_of(c, q, l)
                a, b = GROUPS[g][0], GROUPS[g + groups - 1][1]
                if not (c is None and g0 + g + groups <= RING):
                    dve.wait_ge(s_used, g0 + g + groups - RING)
                slot = (sg + g) % RING
                if g == 0:
                    dve.wait_ge(s_x[l], step + 1)
                for part, first_tile in enumerate(PAIRS[:-1]):
                    if l == 1 and a <= first_tile < b:
                        dve.wait_ge(s_pair[parity][part], 16 * (step + 2 - parity))
                nc.vector.tensor_tensor(ring[:, slot * GT:slot * GT + b - a, :], x0_pair[:, parity, a:b, :],
                                        x_dup[l][:, :].unsqueeze(1).to_broadcast([S, b - a, N]),
                                        ALU.mult).then_inc(s_prod, groups)

            def low_parts(l, g, c, q):
                _, k0 = start_of(c, q, l)
                sg, sk = slot_of(c, q, l)
                k = SPLIT[l].index(g)
                a, b = GROUPS[g]
                n = S
                slot = (sg + g) % RING
                dve.wait_ge(s_hi, k0 + k + 1)
                if g == TAIL:
                    hs = (sk + k) % HRING
                    nc.vector.tensor_tensor(high[HALF:S, hs, 0, :], prod[0:LASTT, slot, b - 1 - a, :],
                                            high[0:LASTT, hs, 0, :].bitcast(FP32), ALU.subtract).then_inc(s_lo, 1)
                    return
                nc.vector.tensor_tensor(low[0:n, slot, 0:b - a, :], prod[0:n, slot, 0:b - a, :],
                                        high[0:n, (sk + k) % HRING, 0:b - a, :].bitcast(FP32), ALU.subtract).then_inc(s_lo, 1)

            def sum_direct(l, src, dst, step, count):
                dve.wait_ge(s_d[l], step + (2 if l == 2 else 1))
                nc.vector.tensor_reduce(dst[:, bass.ds(SB * step, SB)], src.rearrange("p (d b) -> p b d", d=D),
                                        AX.X, ALU.add).then_inc(count, 1)

            def flow(layers, c, q):
                due = []
                for l in layers:
                    if l == 0:
                        continue
                    step, parity = step_of(c, q, l), q % 2
                    g = 0
                    while g < NG:
                        groups = 2 if g in TWICE[l] else 1
                        products(l, g, groups, c, q, step, parity)
                        for at in due:
                            low_parts(*at, c, q)
                        due = [(l, x) for x in range(g, g + groups) if x in SPLIT[l]]
                        g += groups
                        if l == 2 and g == SUM01_AT:
                            sum_direct(1, direct01[:, parity, :], logit01, step, s_sum01)
                        if l == 1 and g == SUM2_AT and c is not None:
                            sum_direct(2, direct2[:, :], logit2, step - 2, s_sum2)
                        if layers == (2,) and q == QS - 1 and g == SUM2_AT:
                            sum_direct(2, direct2[:, :], logit2, step - 1, s_sum2)
                if layers == (2,) and q == QS - 1:
                    sum_direct(2, direct2[:, :], logit2, step, s_sum2)

            flow((0, 1), None, 0)
            flow((0, 1), None, 1)

            def body(c, q):
                flow(layers_of(c, q), c, q)

            with dve.Fori(0, CHUNKS - 1) as c:
                for q in range(QS):
                    body(c, q)
            for q in range(QS):
                body(CHUNKS - 1, q)


def kernel(dense_ctx, ids, W_top1, b_top1, W_top2, b_top2, W_top3,
           L0_rec_w0, L0_rec_w1, L0_rec_w2, L0_rec_b0, L0_rec_b1, L0_rec_b2, **tables):
    import numpy as np
    import concourse.bacc as bacc
    from concourse.bass_utils import run_bass_kernel_spmd

    nc = bacc.Bacc("TRN2", target_bir_lowering=False, num_devices=1)
    arrays = {}

    def given(name, a):
        arrays[name] = np.ascontiguousarray(a)
        return nc.dram_tensor(name, arrays[name].shape, mybir.dt.from_np(arrays[name].dtype), kind="ExternalInput").ap()

    h = np.tile(np.arange(F), SHIFTS)
    k = (h + np.repeat(np.arange(SHIFTS), F)) % F
    w0 = np.asarray(L0_rec_w0)
    args = [given("dense_ctx", dense_ctx), given("ids", ids), [given(f"tbl_{f}", tables[f"tbl_{f}"]) for f in range(F)],
            given("w0_hk", w0[h, k]), given("w0_kh", w0[k, h]), given("w1", L0_rec_w1), given("w2", L0_rec_w2),
            [given("b0", L0_rec_b0), given("b1", L0_rec_b1), given("b2", L0_rec_b2)],
            given("w_top1", W_top1), given("b_top1", b_top1), given("w_top2", W_top2), given("b_top2", b_top2),
            given("w_top3", W_top3), given("identity", np.eye(128, dtype=np.float32))]
    out = nc.dram_tensor("y", (B, 1), FP32, kind="ExternalOutput").ap()
    build(nc, *args, out)
    r = run_bass_kernel_spmd(nc, [arrays], core_ids=[0])
    return r.results[0]["y"]
```

```python
import concourse.bass as bass
from concourse import mybir

FP32 = mybir.dt.float32
FP32R = mybir.dt.float32r
I32 = mybir.dt.int32
ALU = mybir.AluOpType
ACT = mybir.ActivationFunctionType
AX = mybir.AxisListType

B, F, D, S = 1024, 39, 16, 128
HALF = S // 2
CHUNK = 128
CHUNKS = B // CHUNK
QS = 4
SB = CHUNK // QS
N = SB * D
STEPS = CHUNKS * QS
SHIFTS = (F + 1) // 2
SLOTS = S // F
ROWS0 = SLOTS * F
TILES0 = -(-SHIFTS // SLOTS)
LAST0 = (SHIFTS - SLOTS * (TILES0 - 1)) * F
TILES = (F + 1) // 2
LASTT = (F - 2 * (TILES - 1)) * HALF
GT = 2
GROUPS = [(a, a + GT) for a in (*range(0, TILES - 2 * GT, GT), TILES - GT, TILES - 2 * GT)]
NG = len(GROUPS)
TAIL = NG - 2
SPLIT = {1: (2, 3, 5, 6, 7, TAIL), 2: (0, 2, 4, 5, 6, 7, TAIL)}
TWICE = {1: (0, 2, 4, 6), 2: (2, 4, 6)}
POOL_LOWS = {1: (3,), 2: (5,)}
LAST_POOL_LOWS = (0, 2, 5, 7)
POOL_GROUPS = [(0, 4), (4, TILES0)]
G_FIRST = 2 * NG
G_STEP = 2 * NG
K_FIRST = 2 * len(SPLIT[1])
K_STEP = len(SPLIT[1]) + len(SPLIT[2])
GATHERS = (4, 11, 12, 12)
FIRST_GATHERS = (10, 24)
COPY_AT = 3
STORE_AT = (1, 2, 2)
POOL0_AT = (3, 4)
PAIRS = (0, 4, 8, 12, TILES)
RELU0_AT = 5
RELU2_AT = 7
TR_AT = 0
SUM2_AT = 9
SUM01_AT = 2
RING = 8
HRING = 4
J1, J2, DENSE = 512, 256, 16
DENSE_AT = (0, 32, 64)
DROWS = DENSE_AT[-1] + DENSE
DENSE_AFTER = 5
MN = 512


def rows_of(layer, tile):
    if layer == 0:
        return LAST0 if tile == TILES0 - 1 else ROWS0
    return LASTT if tile == TILES - 1 else S


def is_split(layer, t):
    if layer == 0:
        return False
    g = next(g for g, (a, b) in enumerate(GROUPS) if a <= t < b)
    return g in SPLIT[layer] and (g != TAIL or t == TILES - 1)


def tile_at(layer, t):
    before = [(l, x) for l in range(3) for x in range(TILES if l else TILES0)]
    before = before[:before.index((layer, t))]
    return sum(is_split(*x) == is_split(layer, t) for x in before)


def build(nc, dense, ids, tables, wa, wb, w1, w2, biases, wt1, bt1, wt2, bt2, wt3, ident, out):
    def sb(name, shape, dt=FP32):
        return nc.alloc_sbuf_tensor(name, shape, dt)

    sem = nc.alloc_semaphore

    x0_dram = nc.dram_tensor("x0_scratch", [STEPS, 2 * F, N], FP32).ap()

    ids_all = sb("ids_all", [CHUNK, CHUNKS, F], I32)
    ids_now = sb("ids_now", [CHUNK, F], I32)
    emb = sb("emb", [CHUNK, F * D])
    x0t = sb("x0t", [F, QS, D, SB])
    eye = sb("eye", [128, 128])
    x0_rep = sb("x0_rep", [ROWS0, N])
    x0_shift = sb("x0_shift", [ROWS0, TILES0, N])
    pair_ptr = nc.sbuf_base
    x0_pair = sb("x0_pair", [S, 2, TILES, N])
    direct01 = sb("direct01", [S, 2, N])
    direct2 = sb("direct2", [S, N])
    logit01 = sb("logit01", [S, B])
    logit2 = sb("logit2", [S, B])
    prod_ptr = nc.sbuf_base
    prod = sb("prod", [S, RING, GT, N])
    low = nc.alloc_sbuf_tensor_at("low", [S, RING, GT, N], FP32R, offset=prod_ptr)
    high = sb("high", [S, HRING, GT, N], FP32R)
    kinds = [is_split(l, t) for l in range(3) for t in range(TILES if l else TILES0)]
    n32, nsp = kinds.count(False), kinds.count(True)
    w_32 = sb("w_32", [S, n32, S])
    w_hi = sb("w_hi", [S, nsp, S], FP32R)
    w_lo = sb("w_lo", [S, nsp, S], FP32R)
    bias = sb("bias", [S, 3])
    bias_t1 = sb("bias_t1", [128, J1 // 128])
    bias_t2 = sb("bias_t2", [128, J2 // 128])
    w_t3 = sb("w_t3", [128, J2 // 128])

    stage = prod[:, :, :, :].rearrange("p r g n -> p (r g n)").rearrange("p (t s) -> p t s", s=S)
    STAGE = {0: 0, 1: 2 * TILES0, 2: 2 * TILES0 + TILES}
    pair_parts = nc.alloc_sbuf_tensor_at("pair_parts", [S, 2, TILES, N], FP32R, offset=pair_ptr)
    used = 0

    def even(cols, parts=False):
        nonlocal used
        used += cols
        assert used <= TILES * N
        buf = pair_parts if parts else x0_pair
        return buf[:, 0, :, :].rearrange("p t n -> p (t n)")[:, used - cols:used]

    w_t1 = even(3 * J1).rearrange("p (k j) -> p k j", k=3)
    w_t2 = even(4 * J2).rearrange("p (k j) -> p k j", k=4)
    w_t1_hi = even(3 * J1, True).rearrange("p (k j) -> p k j", k=3)
    w_t1_lo = even(2 * J1, True).rearrange("p (k j) -> p k j", k=2)
    w_t2_hi = even(4 * J2, True).rearrange("p (k j) -> p k j", k=4)
    w_t2_lo = even(4 * J2, True).rearrange("p (k j) -> p k j", k=4)
    dense_in = even(CHUNKS * DROWS).rearrange("p (c f) -> p c f", f=DROWS)
    y_row = even(B)[0:1, :]
    dense_t = even(B, True)[0:DROWS, :]
    odd = x0_pair[:, 1, :, :].rearrange("p t n -> p (t n)")
    odd_parts = pair_parts[:, 1, :, :].rearrange("p t n -> p (t n)")
    h1 = odd[:, 0:4 * B].rearrange("p (m b) -> p m b", m=4)
    h2 = odd[:, 4 * B:6 * B].rearrange("p (m b) -> p m b", m=2)
    logit_hi = odd_parts[:, 6 * B:8 * B].rearrange("p (k b) -> p k b", k=2)
    logit_lo = odd_parts[:, 8 * B:10 * B].rearrange("p (k b) -> p k b", k=2)
    h1_hi = high[:, :, :, :].rearrange("p r g n -> p (r g n)")[:, 0:4 * B].rearrange("p (m b) -> p m b", m=4)
    h1_lo = low[:, :, :, :].rearrange("p r g n -> p (r g n)")[:, 0:4 * B].rearrange("p (m b) -> p m b", m=4)

    z_ps = {l: nc.alloc_psum_tensor(f"z{l}_ps", [S, N], FP32) for l in range(3)}
    tr_ps = [nc.alloc_psum_tensor(f"tr{i}_ps", [S, N], FP32) for i in range(2)]
    x_dup = {l: nc.alloc_psum_tensor(f"x{l}_dup", [S, N], FP32) for l in (1, 2)}
    mlp_ps = list(z_ps.values())
    MR = len(mlp_ps)

    s_ids, s_idsc, s_eye, s_dense = sem("ids_loaded"), sem("ids_copied"), sem("eye_loaded"), sem("dense_loaded")
    s_w, s_bias, s_wz = sem("weights_loaded"), sem("biases_loaded"), sem("weights_zeroed")
    s_xz = sem("x0_pads_zeroed")
    s_ws, s_wp = sem("weights_summed"), sem("weights_ready")
    s_emb = sem("emb_gathered")
    s_tr, s_trc, s_scr = sem("transposed"), sem("transposes_copied"), sem("x0_stored")
    s_shift = sem("shifts_loaded")
    s_pair = [[sem(f"pairs_loaded_{p}_{part}") for part in range(len(PAIRS) - 1)] for p in ("even", "odd")]
    s_prod0, s_used0 = sem("layer0_products_ready"), sem("layer0_products_used")
    s_prod, s_used = sem("products_ready"), sem("products_used")
    s_hi, s_lo, s_lo_pool = sem("high_ready"), sem("low_ready_dve"), sem("low_ready_pool")
    s_z = {l: sem(f"z{l}_ready") for l in range(3)}
    s_x = {1: sem("x1_ready"), 2: sem("x2_ready")}
    s_d = {l: sem(f"direct{l}_ready") for l in range(3)}
    s_sum01, s_sum2 = sem("direct01_summed"), sem("direct2_summed")
    s_wt = sem("mlp_weights_loaded")
    s_mz, s_dtr = sem("mlp_zeros_ready"), sem("dense_transposed")
    s_mhi, s_mlo = sem("mlp_high_ready"), sem("mlp_low_ready")
    s_h1hi, s_h1lo = sem("h1_high_ready"), sem("h1_low_ready")
    s_m, s_mr = sem("mlp_product_ready"), sem("mlp_relu_done")
    s_out = sem("y_stored")
    s_pe_note, s_pool_note = sem("transposes_begun"), sem("gathers_begun")
    s_sp_note = sem("chunk_loads_begun")

    def layers_of(c, q):
        if c is None:
            return (0, 1)
        return (2,) if q >= QS - 2 and isinstance(c, int) and c == CHUNKS - 1 else (0, 2, 1)

    def number(c, q, layer, n):
        if c is None:
            return n[1] * q
        total = 2 * n[1] + (n[1] + n[2]) * q + (n[1] + n[2]) * QS * c
        if isinstance(c, int) and c == CHUNKS - 1 and q == QS - 1:
            return total - n[1]
        return total + n[2] if layer == 1 else total

    def start_of(c, q, layer):
        return number(c, q, layer, {1: NG, 2: NG}), number(c, q, layer, {l: len(SPLIT[l]) for l in (1, 2)})

    def lows_of(c, q, layer, by_pool):
        pool_lows = LAST_POOL_LOWS if c is not None and layers_of(c, q) == (2,) else POOL_LOWS[layer]
        return [g for g in SPLIT[layer] if (g in pool_lows) == by_pool]

    def lows_ready(c, q, layer, g):
        by_pool = g in lows_of(c, q, layer, True)
        same = {l: len(lows_of(None, 0, l, by_pool)) for l in (1, 2)}
        if isinstance(c, int) and c == CHUNKS - 1 and q == QS - 1:
            before = number(c, QS - 2, layer, same) + len(lows_of(c, QS - 2, layer, by_pool))
        else:
            before = number(c, q, layer, same)
        return s_lo_pool if by_pool else s_lo, before + lows_of(c, q, layer, by_pool).index(g) + 1

    def step_of(c, q, layer):
        return q if c is None else QS * c + (q + (0 if layer == 2 else 2))

    def slot_of(c, q, layer):
        return start_of(c if c is None or layers_of(c, q) == (2,) else 0, q, layer)

    block = nc.Block()
    with block:

        @block.sync
        def _(sp):
            sp.dma_start(ids_all[:, :, :], ids.rearrange("(c p) f -> p c f", p=CHUNK)).then_inc(s_ids, 16)
            sp.dma_start(eye[:, :], ident).then_inc(s_eye, 16)
            sp.wait_ge(s_wz, 1)
            full = ROWS0 * (TILES0 - 1)
            sp.dma_start(stage[0:ROWS0, 0:TILES0 - 1, :],
                         wa[0:full, :].rearrange("(t p) s -> p t s", p=ROWS0)).then_inc(s_w, 16)
            sp.dma_start(stage[0:LAST0, TILES0 - 1, :], wa[full:full + LAST0, :]).then_inc(s_w, 16)
            sp.dma_start(stage[F:ROWS0, TILES0, :], wb[F:ROWS0, :]).then_inc(s_w, 16)
            sp.dma_start(stage[0:ROWS0, TILES0 + 1:2 * TILES0 - 1, :],
                         wb[ROWS0:full, :].rearrange("(t p) s -> p t s", p=ROWS0)).then_inc(s_w, 16)
            sp.dma_start(stage[0:LAST0, 2 * TILES0 - 1, :], wb[full:full + LAST0, :]).then_inc(s_w, 16)
            for l, w in ((1, w1), (2, w2)):
                flat = w.rearrange("h k s -> (h k) s")
                n = S * (TILES - 1)
                sp.dma_start(stage[:, STAGE[l]:STAGE[l] + TILES - 1, :],
                             flat[0:n, :].rearrange("(t p) s -> p t s", p=S)).then_inc(s_w, 16)
                sp.dma_start(stage[0:LASTT, STAGE[l] + TILES - 1, :], flat[n:n + LASTT, :]).then_inc(s_w, 16)

            def row(i, r):
                return x0_dram[i, r, :]

            def load_shifts(i):
                for j in range(SLOTS):
                    tiles = len(range(j, SHIFTS, SLOTS))
                    at = row(i, j)
                    sp.dma_start(x0_shift[j * F:(j + 1) * F, 0:tiles, :],
                                 bass.AP(at.tensor, at.offset, [[N, F], [SLOTS * N, tiles], [1, N]])).then_inc(s_shift, 16)
                    sp.dma_start(x0_rep[j * F:(j + 1) * F, :], x0_dram[i, 0:F, :]).then_inc(s_shift, 16)

            def load_pairs(i, parity):
                for part, (t0, t1) in enumerate(zip(PAIRS, PAIRS[1:])):
                    if not (isinstance(i, int) and i < 2):
                        sp.wait_ge(s_prod, G_STEP * i + (G_FIRST - 2 * G_STEP + (NG if t1 == TILES else t1 // GT)))
                    for j in range(2):
                        tiles = len(range(2 * t0 + j, min(2 * t1, F), 2))
                        at = row(i, 2 * t0 + j)
                        sp.dma_start(x0_pair[j * HALF:(j + 1) * HALF, parity, t0:t0 + tiles, :],
                                     bass.AP(at.tensor, at.offset, [[0, HALF], [2 * N, tiles], [1, N]])
                                     ).then_inc(s_pair[parity][part], 16)

            def chunk(c):
                sp.wait_ge(s_scr, 32 * (c + 1))
                sp.sem_inc(s_sp_note, 1)
                for q in range(QS):
                    i = QS * c + q
                    if not (isinstance(c, int) and i == 0):
                        sp.wait_ge(s_used0, i)
                    load_shifts(i)
                    load_pairs(i, q % 2)

            sp.wait_ge(s_xz, 1)
            chunk(0)
            with sp.Fori(1, CHUNKS) as c:
                chunk(c)

            sp.wait_ge(s_mz, 1)
            for at in DENSE_AT:
                sp.dma_start(dense_in[:, :, at:at + DENSE], dense.rearrange("(c p) f -> p c f", p=CHUNK)).then_inc(s_dense, 16)
            sp.dma_start(w_t1[:, 0:2, :], wt1[0:2 * S, :].rearrange("(k p) j -> p k j", p=S)).then_inc(s_wt, 16)
            for at in DENSE_AT:
                sp.dma_start(w_t1[at:at + DENSE, 2, :], wt1[2 * S:2 * S + DENSE, :]).then_inc(s_wt, 16)
            sp.dma_start(w_t2, wt2.rearrange("(k p) j -> p k j", p=128)).then_inc(s_wt, 16)
            sp.wait_ge(s_mr, 2 * 4 + 2 * 2 + 2)
            sp.dma_start(out.rearrange("b o -> o b"), y_row[:, :]).then_inc(s_out, 16)
            sp.wait_ge(s_out, 16)

        @block.gpsimd
        def _(pool):
            pool.wait_ge(s_ids, 16)

            def indices(c):
                nc.gpsimd.tensor_copy(ids_now[:, :], ids_all[:, c, :]).then_inc(s_idsc, 1)
                pool.wait_ge(s_idsc, c + 1)
                pool.sem_inc(s_pool_note, 1)

            def gather(f0, f1):
                for f in range(f0, f1):
                    pool.indirect_dma_start(emb[:, f * D:(f + 1) * D], None, tables[f][:, :],
                                            bass.IndirectOffsetOnAxis(ap=ids_now[:, f:f + 1], axis=0)).then_inc(s_emb, 16)

            def store(c):
                pool.wait_ge(s_trc, QS * (c + 1))
                for half in range(2):
                    dst = x0_dram[bass.ds(QS * c, QS), half * F:(half + 1) * F, :]
                    pool.dma_start(dst.rearrange("q f n -> f q n"),
                                   x0t[:, :, :, :].rearrange("f q d b -> f q (d b)")).then_inc(s_scr, 16)

            def products0(step, part):
                if part == 0:
                    pool.wait_ge(s_shift, 2 * SLOTS * 16 * (step + 1))
                a, b = POOL_GROUPS[part]
                nc.gpsimd.tensor_tensor(x0_shift[:, a:b, :], x0_shift[:, a:b, :],
                                        x0_rep[:, :].unsqueeze(1).to_broadcast([ROWS0, b - a, N]),
                                        ALU.mult).then_inc(s_prod0, 1)

            def low_parts(l, g, c, q):
                sg, sk = slot_of(c, q, l)
                k = SPLIT[l].index(g)
                slot = (sg + g) % RING
                pool.wait_ge(s_hi, start_of(c, q, l)[1] + k + 1)
                nc.gpsimd.tensor_tensor(low[:, slot, :, :], prod[:, slot, :, :],
                                        high[:, (sk + k) % HRING, :, :].bitcast(FP32), ALU.subtract).then_inc(s_lo_pool, 1)

            def body(c, q, f0, f1, next_step=None):
                slots = [(l, g) for l in layers_of(c, q) if l for g in range(NG)]
                for n, (l, g) in enumerate(slots):
                    if g in lows_of(c, q, l, True):
                        low_parts(l, g, c, q)
                    if (q, l, g) == STORE_AT and c is not None and not (
                            isinstance(c, int) and c == CHUNKS - 1):
                        store(c + 1)
                    if l == 1 and g in POOL0_AT and next_step is not None:
                        products0(next_step, POOL0_AT.index(g))
                    gather(f0 + (f1 - f0) * n // len(slots), f0 + (f1 - f0) * (n + 1) // len(slots))

            def chunk(c):
                at = 0 if isinstance(c, int) and c == CHUNKS - 1 else F - sum(GATHERS[:TR_AT + 1])
                for q in range(QS):
                    if isinstance(c, int) and (c == CHUNKS - 1 or c == CHUNKS - 2 and q > TR_AT):
                        n = 0
                    else:
                        n = GATHERS[q]
                    if q == TR_AT + 1:
                        at = 0
                        if n:
                            pool.wait_ge(s_tr, QS * (c + 2))
                            pool.wait_ge(s_emb, 16 * F * (c + 2))
                            indices(c + 2)
                    if q == TR_AT:
                        gather(at, at + n)
                        at, n = at + n, 0
                    k = QS * c + (q + 3)
                    body(c, q, at, at + n, None if isinstance(k, int) and k >= STEPS else k)
                    at += n

            indices(0)
            gather(0, F)
            store(0)
            pool.wait_ge(s_tr, QS)
            pool.wait_ge(s_emb, 16 * F)
            indices(1)
            gather(0, FIRST_GATHERS[0])
            body(None, 0, *FIRST_GATHERS, 1)
            body(None, 1, FIRST_GATHERS[1], F - sum(GATHERS[:TR_AT + 1]), 2)
            with pool.Fori(0, CHUNKS - 2) as c:
                chunk(c)
            chunk(CHUNKS - 2)
            chunk(CHUNKS - 1)

        @block.tensor
        def _(pe):
            def transposes(c):
                pe.wait_ge(s_emb, 16 * F * (c + 1))
                rows = emb[:, :].rearrange("b (f d) -> b d f", d=D)
                for r in range(4):
                    if not (isinstance(c, int) and c == 0 and r < 2):
                        pe.wait_ge(s_trc, 4 * c + r - 1)
                    pe.sem_inc(s_pe_note, 1)
                    for d in range(4):
                        last = nc.tensor.transpose(tr_ps[r % 2][0:F, d * CHUNK:(d + 1) * CHUNK],
                                                   rows[:, 4 * r + d, :], eye[:, :])
                    last.then_inc(s_tr, 1)

            def dense_transposes():
                pe.wait_ge(s_dense, 48)
                for r in range(2):
                    for j in range(4):
                        last = nc.tensor.transpose(tr_ps[r][0:DROWS, j * CHUNK:(j + 1) * CHUNK],
                                                   dense_in[:, 4 * r + j, :], eye[:, :])
                    last.then_inc(s_dtr, 1)

            def layer(l, c, q, step):
                g0, k0 = start_of(c, q, l)
                sg, sk = slot_of(c, q, l)
                if l == 2:
                    pe.wait_ge(s_d[l], step + 1)
                elif not (isinstance(step, int) and step == 0):
                    pe.wait_ge(s_d[l], step)
                if l == 0:
                    for g, (a, b) in enumerate(POOL_GROUPS):
                        pe.wait_ge(s_prod0, len(POOL_GROUPS) * step + g + 1)
                        for t in range(a, b):
                            n = rows_of(l, t)
                            last = nc.tensor.matmul(z_ps[l][:, :], w_32[0:n, tile_at(l, t), :], x0_shift[0:n, t, :],
                                                    start=(t == 0), stop=(t == TILES0 - 1))
                    last.then_inc(s_used0, 1)
                    return
                k = 0
                left = sum((3 if rows_of(l, t) > HALF else 2) if is_split(l, t) else 1
                           for t in range(TILES))
                first = [True]

                def product(w, p):
                    nonlocal left
                    left -= 1
                    last = nc.tensor.matmul(z_ps[l][:, :], w, p, start=first[0], stop=(left == 0))
                    first[0] = False
                    return last

                for g, (a, b) in enumerate(GROUPS):
                    slot = (sg + g) % RING
                    if g in SPLIT[l]:
                        hslot = (sk + k) % HRING
                        if g == TAIL:
                            pe.wait_ge(s_prod, g0 + g + 1)
                            for t in range(a, b - 1):
                                product(w_32[0:rows_of(l, t), tile_at(l, t), :], prod[0:rows_of(l, t), slot, t - a, :])
                            at = tile_at(l, b - 1)
                            pe.wait_ge(s_hi, k0 + k + 1)
                            product(w_lo[0:LASTT, at, :], high[0:LASTT, hslot, 0, :])
                            pe.wait_ge(*lows_ready(c, q, l, g))
                            last = product(w_hi[:, at, :], high[:, hslot, 0, :])
                        else:
                            pe.wait_ge(s_hi, k0 + k + 1)
                            for t in range(a, b):
                                n, at = rows_of(l, t), tile_at(l, t)
                                product(w_hi[0:n, at, :], high[0:n, hslot, t - a, :])
                                product(w_lo[0:n, at, :], high[0:n, hslot, t - a, :])
                            pe.wait_ge(*lows_ready(c, q, l, g))
                            for t in range(a, b):
                                n, at = rows_of(l, t), tile_at(l, t)
                                last = product(w_hi[0:n, at, :], low[0:n, slot, t - a, :])
                        k += 1
                    else:
                        pe.wait_ge(s_prod, g0 + g + 1)
                        for t in range(a, b):
                            n, at = rows_of(l, t), tile_at(l, t)
                            last = product(w_32[0:n, at, :], prod[0:n, slot, t - a, :])
                    last.then_inc(s_used, 1)
                    if l == 2 and g == DENSE_AFTER and isinstance(step, int) and step == STEPS - 1:
                        dense_transposes()

            pe.wait_ge(s_eye, 16)
            transposes(0)
            pe.wait_ge(s_wp, 1)
            for step in range(2):
                layer(0, None, step, step)
                layer(1, None, step, step)

            def body(c, q):
                for l in layers_of(c, q):
                    layer(l, c, q, step_of(c, q, l))
                    if l == 2 and q == TR_AT and not (isinstance(c, int) and c == CHUNKS - 1):
                        transposes(c + 1)

            with pe.Fori(0, CHUNKS - 1) as c:
                for q in range(QS):
                    body(c, q)
            for q in range(QS - 1):
                body(CHUNKS - 1, q)
            body(CHUNKS - 1, QS - 1)

            def in_parts(ps, w, x, first=False, stop=False):
                nc.tensor.matmul(ps, w[0], x[0], start=first, stop=False)
                nc.tensor.matmul(ps, w[0], x[1], start=False, stop=False)
                return nc.tensor.matmul(ps, w[1], x[0], start=False, stop=stop)

            n = 0
            for nb in range(B // MN):
                cols = slice(nb * MN, (nb + 1) * MN)
                pe.wait_ge(s_mlo, 7 + nb)
                for m in range(J1 // 128):
                    if n == 2:
                        pe.wait_ge(s_d[2], STEPS + 1)
                    if n >= MR:
                        pe.wait_ge(s_mr, n - MR + 1)
                    ps = mlp_ps[n % MR][:, :]
                    js = slice(m * 128, (m + 1) * 128)
                    for k in range(2):
                        in_parts(ps, (w_t1_hi[:, k, js], w_t1_lo[:, k, js]),
                                 (logit_hi[:, k, cols], logit_lo[:, k, cols]), first=(k == 0))
                    nc.tensor.matmul(ps, w_t1_hi[0:DROWS, 2, js], dense_t[:, cols],
                                     start=False, stop=True).then_inc(s_m, 1)
                    n += 1
            for nb in range(B // MN):
                cols = slice(nb * MN, (nb + 1) * MN)
                pe.wait_ge(s_h1lo, 4 * (nb + 1))
                for m in range(J2 // 128):
                    pe.wait_ge(s_mr, n - MR + 1)
                    js = slice(m * 128, (m + 1) * 128)
                    for k in range(4):
                        last = in_parts(mlp_ps[n % MR][:, :], (w_t2_hi[:, k, js], w_t2_lo[:, k, js]),
                                        (h1_hi[:, k, cols], h1_lo[:, k, cols]), first=(k == 0), stop=(k == 3))
                    last.then_inc(s_m, 1)
                    n += 1
            for nb in range(B // MN):
                cols = slice(nb * MN, (nb + 1) * MN)
                pe.wait_ge(s_mr, 8 + 2 * (nb + 1))
                pe.wait_ge(s_mr, n - MR + 1)
                for k in range(2):
                    last = nc.tensor.matmul(mlp_ps[n % MR][0:1, :], w_t3[:, k:k + 1], h2[:, k, cols],
                                            start=(k == 0), stop=(k == 1))
                last.then_inc(s_m, 1)
                n += 1

        @block.scalar
        def _(act):
            with nc.allow_non_contiguous_dma("one column of biases"):
                for l in range(3):
                    act.dma_start(bias[:, l:l + 1], biases[l].unsqueeze(1)).then_inc(s_bias, 16)
                act.dma_start(bias_t1[:, :], bt1.rearrange("(m p) -> p m", p=128)).then_inc(s_bias, 16)
                act.dma_start(bias_t2[:, :], bt2.rearrange("(m p) -> p m", p=128)).then_inc(s_bias, 16)
                act.dma_start(w_t3[:, :], wt3.rearrange("(m p) o -> p (m o)", p=128)).then_inc(s_bias, 16)

            def copy_transposes(c):
                if not (isinstance(c, int) and c == 0):
                    act.wait_ge(s_scr, 32 * c)
                for r in range(4):
                    act.wait_ge(s_tr, 4 * c + r + 1)
                    nc.scalar.copy(x0t[:, :, 4 * r:4 * r + 4, :],
                                   tr_ps[r % 2][0:F, :].rearrange("f (d q b) -> f q d b", d=4, q=QS)).then_inc(s_trc, 1)

            def round_high(l, g, c, q):
                g0, k0 = start_of(c, q, l)
                sg, sk = slot_of(c, q, l)
                k = SPLIT[l].index(g)
                a, b = GROUPS[g]
                n = S
                act.wait_ge(s_prod, g0 + g + 1)
                if not (c is None and sk + k < HRING):
                    act.wait_ge(s_used, g0 + g - groups_back(c, q, l, g, HRING) + 1)
                if g == TAIL:
                    nc.scalar.copy(high[0:LASTT, (sk + k) % HRING, 0, :],
                                   prod[0:LASTT, (sg + g) % RING, b - 1 - a, :]).then_inc(s_hi, 1)
                else:
                    nc.scalar.copy(high[0:n, (sk + k) % HRING, 0:b - a, :],
                                   prod[0:n, (sg + g) % RING, 0:b - a, :]).then_inc(s_hi, 1)

            def groups_back(c, q, l, g, back):
                before = (1,) * q if c is None else (1, 2) if q == QS - 1 and layers_of(c, q) == (2,) else (1,)
                order = [(y, x) for y in before + layers_of(c, q) if y for x in range(NG)]
                here = at = max(n for n, x in enumerate(order) if x == (l, g))
                while back:
                    at -= 1
                    back -= order[at][1] in SPLIT[order[at][0]]
                assert at >= 0
                return here - at

            def relus(l, step, parity, groups=None):
                if l == 0:
                    act.wait_ge(s_used0, step + 1)
                else:
                    act.wait_ge(s_used, groups)
                first = isinstance(step, int) and step == 0
                if l < 2:
                    if not first:
                        act.wait_ge(s_prod, NG if l == 0 and isinstance(step, int) and step == 1
                                    else G_STEP * step + (G_FIRST + (-2 * G_STEP if l == 0 else NG - G_STEP)))
                    nc.scalar.activation(x_dup[l + 1][0:HALF, :], z_ps[l][0:HALF, :], ACT.Relu, bias=bias[0:HALF, l:l + 1])
                    nc.scalar.activation(x_dup[l + 1][HALF:S, :], z_ps[l][0:HALF, :], ACT.Relu,
                                         bias=bias[0:HALF, l:l + 1]).then_inc(s_x[l + 1], 1)
                    act.wait_ge(s_sum01, step + 1)
                    nc.scalar.activation(direct01[l * HALF:(l + 1) * HALF, parity, :], z_ps[l][HALF:S, :], ACT.Relu,
                                         bias=bias[HALF:S, l:l + 1]).then_inc(s_d[l], 1)
                else:
                    act.wait_ge(s_sum2, step + 1)
                    nc.scalar.activation(direct2[:, :], z_ps[l][:, :], ACT.Relu, bias=bias[:, l:l + 1]).then_inc(s_d[l], 1)

            act.wait_ge(s_bias, 96)
            copy_transposes(0)
            relus(0, 0, 0)
            for g in SPLIT[1]:
                round_high(1, g, None, 0)
            relus(1, 0, 0, NG)
            relus(0, 1, 1)
            for g in SPLIT[1]:
                round_high(1, g, None, 1)

            def body(c, q):
                start = start_of(c, q, 2)[0]
                layers = layers_of(c, q)
                for g in range(NG):
                    if g == RELU0_AT and 0 in layers:
                        relus(0, QS * c + (q + 2), q % 2)
                    if g in SPLIT[2]:
                        round_high(2, g, c, q)
                if 1 in layers or q == QS - 2:
                    relus(1, QS * c + (q + 1), (q + 1) % 2, start)
                for g in range(NG if 1 in layers else 0):
                    if g == COPY_AT and q == TR_AT and not (isinstance(c, int) and c == CHUNKS - 1):
                        copy_transposes(c + 1)
                    if g == RELU2_AT:
                        relus(2, QS * c + q, q % 2, start + NG)
                    if g in SPLIT[1]:
                        round_high(1, g, c, q)
                if 1 not in layers and q == QS - 2:
                    relus(2, QS * c + q, q % 2, start + NG)

            with act.Fori(0, CHUNKS - 1) as c:
                for q in range(QS):
                    body(c, q)
            for q in range(QS):
                body(CHUNKS - 1, q)

            act.wait_ge(s_wt, 5 * 16)
            nc.scalar.copy(w_t1_hi[:, 0:2, :], w_t1[:, 0:2, :]).then_inc(s_mhi, 1)
            nc.scalar.copy(w_t1_hi[0:DROWS, 2, :], w_t1[0:DROWS, 2, :]).then_inc(s_mhi, 1)
            nc.scalar.copy(w_t2_hi, w_t2).then_inc(s_mhi, 1)
            for r in range(2):
                act.wait_ge(s_dtr, r + 1)
                nc.scalar.copy(dense_t[:, r * MN:(r + 1) * MN], tr_ps[r][0:DROWS, :]).then_inc(s_mhi, 1)
            groups = start_of(CHUNKS - 1, QS - 1, 2)[0] + NG
            act.wait_ge(s_prod, groups)
            act.wait_ge(s_sum01, STEPS + 2)
            nc.scalar.copy(logit_hi[:, 0, :], logit01[:, :]).then_inc(s_mhi, 1)
            nc.scalar.copy(logit_hi[:, 1, 0:MN], logit2[:, 0:MN]).then_inc(s_mhi, 1)
            relus(2, STEPS - 1, (STEPS - 1) % 2, groups)
            act.wait_ge(s_sum2, STEPS + 1)
            nc.scalar.copy(logit_hi[:, 1, MN:B], logit2[:, MN:B]).then_inc(s_mhi, 1)
            n = 0
            for dst, b_col, m_tiles in ((h1, bias_t1, 4), (h2, bias_t2, 2)):
                for nb in range(B // MN):
                    cols = slice(nb * MN, (nb + 1) * MN)
                    for m in range(m_tiles):
                        act.wait_ge(s_m, n + 1)
                        nc.scalar.activation(dst[:, m, cols], mlp_ps[n % MR][:, :], ACT.Relu,
                                             bias=b_col[:, m:m + 1]).then_inc(s_mr, 1)
                        n += 1
                        if dst is h1:
                            act.wait_ge(s_mr, n)
                            nc.scalar.copy(h1_hi[:, m, cols], h1[:, m, cols]).then_inc(s_h1hi, 1)
            for nb in range(B // MN):
                act.wait_ge(s_m, n + 1)
                nc.scalar.copy(y_row[:, nb * MN:(nb + 1) * MN], mlp_ps[n % MR][0:1, :]).then_inc(s_mr, 1)
                n += 1

        @block.vector
        def _(dve):
            for t in (TILES0 - 1, TILES0):
                nc.vector.memset(stage[:, t, :], 0.0)
            nc.vector.memset(stage[:, 2 * TILES0 - 1, :], 0.0).then_inc(s_sum2, 1)
            nc.vector.memset(stage[:, STAGE[1] + TILES - 1, :], 0.0).then_inc(s_d[2], 1)
            nc.vector.memset(stage[:, STAGE[2] + TILES - 1, :], 0.0).then_inc(s_wz, 1)
            nc.vector.memset(x0_shift[:, TILES0 - 1, :], 0.0).then_inc(s_sum01, 2)
            nc.vector.memset(x0_pair[HALF:S, :, TILES - 1, :], 0.0).then_inc(s_xz, 1)
            dve.wait_ge(s_w, 9 * 16)
            nc.vector.tensor_tensor(stage[0:ROWS0, 0:TILES0, :], stage[0:ROWS0, 0:TILES0, :],
                                    stage[0:ROWS0, TILES0:2 * TILES0, :], ALU.add).then_inc(s_ws, 1)
            dve.wait_ge(s_ws, 1)

            def weights_of(split):
                for l in range(3):
                    n = ROWS0 if l == 0 else S
                    for t in range(TILES if l else TILES0):
                        if is_split(l, t) == split:
                            yield stage[0:n, STAGE[l] + t, :], (slice(0, n), tile_at(l, t))

            for raw, at in weights_of(False):
                nc.vector.tensor_copy(w_32[at], raw)
            for raw, at in weights_of(True):
                last = nc.vector.tensor_copy(w_hi[at], raw)
            last.then_inc(s_ws, 1)
            dve.wait_ge(s_ws, 2)
            for raw, at in weights_of(True):
                last = nc.vector.tensor_tensor(w_lo[at], raw, w_hi[at].bitcast(FP32), ALU.subtract)
            last.then_inc(s_ws, 1)
            dve.wait_ge(s_ws, 3)
            for l in (1, 2):
                at = tile_at(l, TILES - 1)
                last = nc.vector.tensor_copy(w_hi[HALF:S, at, :], w_hi[0:HALF, at, :])
            last.then_inc(s_wp, 1)
            dve.wait_ge(s_wp, 1)

            ring = prod[:, :, :, :].rearrange("p r g n -> p (r g) n")

            def products(l, g, groups, c, q, step, parity):
                g0, _ = start_of(c, q, l)
                sg, _ = slot_of(c, q, l)
                a, b = GROUPS[g][0], GROUPS[g + groups - 1][1]
                if not (c is None and g0 + g + groups <= RING):
                    dve.wait_ge(s_used, g0 + g + groups - RING)
                slot = (sg + g) % RING
                if g == 0:
                    dve.wait_ge(s_x[l], step + 1)
                for part, first_tile in enumerate(PAIRS[:-1]):
                    if l == 1 and a <= first_tile < b:
                        dve.wait_ge(s_pair[parity][part], 16 * (step + 2 - parity))
                nc.vector.tensor_tensor(ring[:, slot * GT:slot * GT + b - a, :], x0_pair[:, parity, a:b, :],
                                        x_dup[l][:, :].unsqueeze(1).to_broadcast([S, b - a, N]),
                                        ALU.mult).then_inc(s_prod, groups)

            def low_parts(l, g, c, q):
                _, k0 = start_of(c, q, l)
                sg, sk = slot_of(c, q, l)
                k = SPLIT[l].index(g)
                a, b = GROUPS[g]
                n = S
                slot = (sg + g) % RING
                dve.wait_ge(s_hi, k0 + k + 1)
                if g == TAIL:
                    hs = (sk + k) % HRING
                    nc.vector.tensor_tensor(high[HALF:S, hs, 0, :], prod[0:LASTT, slot, b - 1 - a, :],
                                            high[0:LASTT, hs, 0, :].bitcast(FP32), ALU.subtract).then_inc(s_lo, 1)
                    return
                nc.vector.tensor_tensor(low[0:n, slot, 0:b - a, :], prod[0:n, slot, 0:b - a, :],
                                        high[0:n, (sk + k) % HRING, 0:b - a, :].bitcast(FP32), ALU.subtract).then_inc(s_lo, 1)

            def sum_direct(l, src, dst, step, count):
                dve.wait_ge(s_d[l], step + (2 if l == 2 else 1))
                nc.vector.tensor_reduce(dst[:, bass.ds(SB * step, SB)], src.rearrange("p (d b) -> p b d", d=D),
                                        AX.X, ALU.add).then_inc(count, 1)

            def flow(layers, c, q):
                due = []
                for l in layers:
                    if l == 0:
                        continue
                    step, parity = step_of(c, q, l), q % 2
                    g = 0
                    while g < NG:
                        groups = 2 if g in TWICE[l] else 1
                        products(l, g, groups, c, q, step, parity)
                        for at in due:
                            low_parts(*at, c, q)
                        due = [(l, x) for x in range(g, g + groups) if x in lows_of(c, q, l, False)]
                        g += groups
                        if l == 2 and g == SUM01_AT:
                            sum_direct(1, direct01[:, parity, :], logit01, step, s_sum01)
                        if l == 1 and g == SUM2_AT and c is not None:
                            sum_direct(2, direct2[:, :], logit2, step - 2, s_sum2)
                        if layers == (2,) and q == QS - 1 and g == SUM2_AT:
                            sum_direct(2, direct2[:, :], logit2, step - 1, s_sum2)

            dve.wait_ge(s_shift, 2 * SLOTS * 16)
            for a, b in POOL_GROUPS:
                nc.vector.tensor_tensor(x0_shift[:, a:b, :], x0_shift[:, a:b, :],
                                        x0_rep[:, :].unsqueeze(1).to_broadcast([ROWS0, b - a, N]),
                                        ALU.mult).then_inc(s_prod0, 1)

            flow((0, 1), None, 0)
            flow((0, 1), None, 1)

            def body(c, q):
                flow(layers_of(c, q), c, q)

            with dve.Fori(0, CHUNKS - 1) as c:
                for q in range(QS):
                    body(c, q)
            for q in range(QS - 1):
                body(CHUNKS - 1, q)
            dve.wait_ge(s_prod, start_of(CHUNKS - 1, QS - 2, 2)[0] + NG)
            nc.vector.memset(w_t1[0:DROWS, 2, :], 0.0)
            nc.vector.memset(dense_in, 0.0).then_inc(s_mz, 1)
            body(CHUNKS - 1, QS - 1)

            def low_part(ready, count, dst, exact, rounded, done):
                dve.wait_ge(ready, count)
                nc.vector.tensor_tensor(dst, exact, rounded.bitcast(FP32), ALU.subtract).then_inc(done, 1)

            a, b, c = (slice(at, at + DENSE) for at in DENSE_AT)
            low_part(s_mhi, 1, w_t1_lo, w_t1[:, 0:2, :], w_t1_hi[:, 0:2, :], s_mlo)
            low_part(s_mhi, 2, w_t1_hi[c, 2, :], w_t1[c, 2, :], w_t1_hi[c, 2, :], s_mlo)
            low_part(s_mhi, 3, w_t2_lo, w_t2, w_t2_hi, s_mlo)
            for r in range(2):
                cols = slice(r * MN, (r + 1) * MN)
                low_part(s_mhi, 4 + r, dense_t[b, cols], tr_ps[r][b, :], dense_t[b, cols], s_mlo)
            low_part(s_mhi, 6, logit_lo[:, 0, :], logit01[:, :], logit_hi[:, 0, :], s_mlo)
            low_part(s_mhi, 7, logit_lo[:, 1, 0:MN], logit2[:, 0:MN], logit_hi[:, 1, 0:MN], s_mlo)
            sum_direct(2, direct2[:, :], logit2, STEPS - 1, s_sum2)
            low_part(s_mhi, 8, logit_lo[:, 1, MN:B], logit2[:, MN:B], logit_hi[:, 1, MN:B], s_mlo)
            n = 0
            for nb in range(B // MN):
                cols = slice(nb * MN, (nb + 1) * MN)
                for m in range(4):
                    n += 1
                    low_part(s_h1hi, n, h1_lo[:, m, cols], h1[:, m, cols], h1_hi[:, m, cols], s_h1lo)


def kernel(dense_ctx, ids, W_top1, b_top1, W_top2, b_top2, W_top3,
           L0_rec_w0, L0_rec_w1, L0_rec_w2, L0_rec_b0, L0_rec_b1, L0_rec_b2, **tables):
    import numpy as np
    import concourse.bacc as bacc
    from concourse.bass_utils import run_bass_kernel_spmd

    nc = bacc.Bacc("TRN2", target_bir_lowering=False, num_devices=1)
    arrays = {}

    def given(name, a):
        arrays[name] = np.ascontiguousarray(a)
        return nc.dram_tensor(name, arrays[name].shape, mybir.dt.from_np(arrays[name].dtype), kind="ExternalInput").ap()

    h = np.tile(np.arange(F), SHIFTS)
    k = (h + np.repeat(np.arange(SHIFTS), F)) % F
    w0 = np.asarray(L0_rec_w0)
    args = [given("dense_ctx", dense_ctx), given("ids", ids), [given(f"tbl_{f}", tables[f"tbl_{f}"]) for f in range(F)],
            given("w0_hk", w0[h, k]), given("w0_kh", w0[k, h]), given("w1", L0_rec_w1), given("w2", L0_rec_w2),
            [given("b0", L0_rec_b0), given("b1", L0_rec_b1), given("b2", L0_rec_b2)],
            given("w_top1", W_top1), given("b_top1", b_top1), given("w_top2", W_top2), given("b_top2", b_top2),
            given("w_top3", W_top3), given("identity", np.eye(128, dtype=np.float32))]
    out = nc.dram_tensor("y", (B, 1), FP32, kind="ExternalOutput").ap()
    build(nc, *args, out)
    r = run_bass_kernel_spmd(nc, [arrays], core_ids=[0])
    return r.results[0]["y"]
```
